# Optimizing a Trainium2 kernel written in Bass

```python
import numpy as np
import jax
import jax.numpy as jnp

def _softmax(x, axis=-1):
    return jax.nn.softmax(x, axis=axis)

def _gelu(x):
    return jax.nn.gelu(x, approximate=True)

def _silu(x):
    return jax.nn.silu(x)

def _sigmoid(x):
    return jax.nn.sigmoid(x)

def _layernorm(x, axis=-1, eps=1e-05):
    m = jnp.mean(x, axis=axis, keepdims=True)
    v = jnp.var(x, axis=axis, keepdims=True)
    return (x - m) / jnp.sqrt(v + eps)

def _scatter_add(tgt, idx, src, axis=0):
    return tgt.at[idx].add(src)

def _segment_sum(src, seg, n):
    return jax.ops.segment_sum(src, seg, n)
kernel_name = 'mk_rec_standalone_d1_rec_r8_72999e'

def setup_inputs(seed: int=0):
    np.random.seed(seed)
    _w = jnp.asarray

    def _rec_inputs():
        import jax
        import jax.numpy as jnp
        _rk = jax.random.key(seed)
        r_ids = jnp.stack([jax.random.randint(jax.random.fold_in(jax.random.fold_in(_rk, 1), 0), (2048,), 449, 999945, jnp.int32), jax.random.randint(jax.random.fold_in(jax.random.fold_in(_rk, 1), 1), (2048,), 18, 999839, jnp.int32), jax.random.randint(jax.random.fold_in(jax.random.fold_in(_rk, 1), 2), (2048,), 611, 999903, jnp.int32), jax.random.randint(jax.random.fold_in(jax.random.fold_in(_rk, 1), 3), (2048,), 200, 999716, jnp.int32), jax.random.randint(jax.random.fold_in(jax.random.fold_in(_rk, 1), 4), (2048,), 1, 999701, jnp.int32), jax.random.randint(jax.random.fold_in(jax.random.fold_in(_rk, 1), 5), (2048,), 64, 999919, jnp.int32), jax.random.randint(jax.random.fold_in(jax.random.fold_in(_rk, 1), 6), (2048,), 28, 999409, jnp.int32), jax.random.randint(jax.random.fold_in(jax.random.fold_in(_rk, 1), 7), (2048,), 49, 999881, jnp.int32), jax.random.randint(jax.random.fold_in(jax.random.fold_in(_rk, 1), 8), (2048,), 81, 999921, jnp.int32), jax.random.randint(jax.random.fold_in(jax.random.fold_in(_rk, 1), 9), (2048,), 341, 999959, jnp.int32), jax.random.randint(jax.random.fold_in(jax.random.fold_in(_rk, 1), 10), (2048,), 145, 999885, jnp.int32), jax.random.randint(jax.random.fold_in(jax.random.fold_in(_rk, 1), 11), (2048,), 1564, 999830, jnp.int32), jax.random.randint(jax.random.fold_in(jax.random.fold_in(_rk, 1), 12), (2048,), 427, 999549, jnp.int32), jax.random.randint(jax.random.fold_in(jax.random.fold_in(_rk, 1), 13), (2048,), 331, 999050, jnp.int32), jax.random.randint(jax.random.fold_in(jax.random.fold_in(_rk, 1), 14), (2048,), 3, 999906, jnp.int32), jax.random.randint(jax.random.fold_in(jax.random.fold_in(_rk, 1), 15), (2048,), 62, 999689, jnp.int32), jax.random.randint(jax.random.fold_in(jax.random.fold_in(_rk, 1), 16), (2048,), 30, 999653, jnp.int32), jax.random.randint(jax.random.fold_in(jax.random.fold_in(_rk, 1), 17), (2048,), 574, 999883, jnp.int32), jax.random.randint(jax.random.fold_in(jax.random.fold_in(_rk, 1), 18), (2048,), 275, 999449, jnp.int32), jax.random.randint(jax.random.fold_in(jax.random.fold_in(_rk, 1), 19), (2048,), 6, 999437, jnp.int32), jax.random.randint(jax.random.fold_in(jax.random.fold_in(_rk, 1), 20), (2048,), 171, 999767, jnp.int32), jax.random.randint(jax.random.fold_in(jax.random.fold_in(_rk, 1), 21), (2048,), 782, 999991, jnp.int32), jax.random.randint(jax.random.fold_in(jax.random.fold_in(_rk, 1), 22), (2048,), 11, 999726, jnp.int32), jax.random.randint(jax.random.fold_in(jax.random.fold_in(_rk, 1), 23), (2048,), 276, 999500, jnp.int32), jax.random.randint(jax.random.fold_in(jax.random.fold_in(_rk, 1), 24), (2048,), 29, 999909, jnp.int32), jax.random.randint(jax.random.fold_in(jax.random.fold_in(_rk, 1), 25), (2048,), 42, 124982, jnp.int32)], axis=1)
        return r_ids
    r_ids = _rec_inputs()

    def _L0_rec_setup():
        import jax, jax.numpy as jnp
        import numpy as np
        B, F, E, H = (512, 26, 64, 125000)
        D = F * E
        key = jax.random.key(seed)
        ks = jax.random.split(key, 12)
        s = 0.02
        return {'ids': jax.random.randint(ks[0], (B, F), 0, H), 'emb': jax.random.normal(ks[1], (H, E), jnp.float32) * s, 'cross_w': jax.random.normal(ks[2], (3, D), jnp.float32) * s, 'cross_b': jnp.zeros((3, D), jnp.float32), 'w1': jax.random.normal(ks[3], (D, 1024), jnp.float32) * s, 'b1': jnp.zeros((1024,), jnp.float32), 'w2': jax.random.normal(ks[4], (1024, 512), jnp.float32) * s, 'b2': jnp.zeros((512,), jnp.float32), 'w3': jax.random.normal(ks[5], (512, 256), jnp.float32) * s, 'b3': jnp.zeros((256,), jnp.float32), 'out_w': jax.random.normal(ks[6], (D + 256, 1), jnp.float32) * s, 'out_b': jnp.zeros((), jnp.float32)}
    _L0_rec_all = _L0_rec_setup()
    _L0_rec_in = {k: v for k, v in _L0_rec_all.items() if k in ('emb', 'cross_w', 'cross_b', 'w1', 'b1', 'w2', 'b2', 'w3', 'b3', 'out_w', 'out_b')}
    del _L0_rec_all
    return {'r_ids': r_ids, 'L0_rec_emb': _L0_rec_in['emb'], 'L0_rec_cross_w': _L0_rec_in['cross_w'], 'L0_rec_cross_b': _L0_rec_in['cross_b'], 'L0_rec_w1': _L0_rec_in['w1'], 'L0_rec_b1': _L0_rec_in['b1'], 'L0_rec_w2': _L0_rec_in['w2'], 'L0_rec_b2': _L0_rec_in['b2'], 'L0_rec_w3': _L0_rec_in['w3'], 'L0_rec_b3': _L0_rec_in['b3'], 'L0_rec_out_w': _L0_rec_in['out_w'], 'L0_rec_out_b': _L0_rec_in['out_b']}

def reference(r_ids, L0_rec_emb, L0_rec_cross_w, L0_rec_cross_b, L0_rec_w1, L0_rec_b1, L0_rec_w2, L0_rec_b2, L0_rec_w3, L0_rec_b3, L0_rec_out_w, L0_rec_out_b):
    import jax
    import jax.numpy as jnp

    def _L0_rec_ref(ids, emb, cross_w, cross_b, w1, b1, w2, b2, w3, b3, out_w, out_b):
        import jax, jax.numpy as jnp
        import numpy as np
        B, F, E, H = (512, 26, 64, 125000)
        D = F * E
        x0 = emb[ids].reshape(ids.shape[0], -1)
        x = x0
        for i in range(cross_w.shape[0]):
            s = x @ cross_w[i]
            x = x0 * s[:, None] + cross_b[i] + x
        h = jax.nn.relu(x0 @ w1 + b1)
        h = jax.nn.relu(h @ w2 + b2)
        h = jax.nn.relu(h @ w3 + b3)
        logit = jnp.concatenate([x, h], axis=1) @ out_w + out_b
        return jax.nn.sigmoid(logit)
    y = _L0_rec_ref(r_ids, L0_rec_emb, L0_rec_cross_w, L0_rec_cross_b, L0_rec_w1, L0_rec_b1, L0_rec_w2, L0_rec_b2, L0_rec_w3, L0_rec_b3, L0_rec_out_w, L0_rec_out_b)
    return y

_drawn_inputs = setup_inputs


def setup_inputs(seed=0):
    import zlib

    import numpy as np

    out = dict(_drawn_inputs(seed))
    spreads = {'L0_rec_cross_b': (0.0, 0.8),
     'L0_rec_b1': (0.0, 0.8),
     'L0_rec_b2': (0.0, 0.8),
     'L0_rec_b3': (0.0, 0.494)}
    factors = {'L0_rec_emb': 8.0,
     'L0_rec_cross_w': 8.0,
     'L0_rec_w1': 8.0,
     'L0_rec_w2': 8.0,
     'L0_rec_w3': 8.0}
    for name, (base, spread) in spreads.items():
        noise = np.random.default_rng([zlib.crc32(name.encode()), seed]).standard_normal(out[name].shape)
        drawn = base * np.exp(spread * noise) if base else spread * noise
        out[name] = jnp.asarray(drawn.astype(out[name].dtype))
    for name, factor in factors.items():
        out[name] = (out[name] * factor).astype(out[name].dtype)
    return out
```

```python
import concourse.bass as bass
from concourse import mybir
from contextlib import ExitStack


def dcn_ranker_kernel(nc, r_ids, emb, cross_w, cross_b, w1, b1, w2, b2, w3, b3, out_w, out_b, out):
    F32 = mybir.dt.float32
    F32R = mybir.dt.float32r
    I32 = mybir.dt.int32
    ALU = mybir.AluOpType
    ACT = mybir.ActivationFunctionType

    P = 128
    B, F = r_ids.shape
    H, E = emb.shape
    D = F * E
    N1, N2, N3 = w1.shape[1], w2.shape[1], w3.shape[1]
    CROSS = cross_w.shape[0]
    TILES = B // P
    K1, K2, K3 = D // P, N1 // P, N2 // P
    VECS = CROSS + 1
    W1C = N1 + VECS
    FPK = P // E
    GK = 4
    GROUPS = [list(range(k, min(k + GK, K1))) for k in range(0, K1, GK)]
    NG = len(GROUPS)
    NF = [len(g) * FPK for g in GROUPS]
    F0 = [g[0] * FPK for g in GROUPS]
    cut = -(-W1C // 3)
    cut += cut % 2
    PIECES = [(0, cut), (cut, W1C - (W1C - cut) // 2), (W1C - (W1C - cut) // 2, W1C)]
    assert all((b - a) % 2 == 0 and 256 <= b - a <= 512 for a, b in PIECES)
    HB = N1 // P // 2
    assert N1 % P == 0 and N2 == 4 * P and N3 <= 512 and NG % 2 == 0 and HB * P <= 512

    STAGE = N1
    W2K, W3K = STAGE // N2, STAGE // N3
    LOADS = [("w1", k, 1) for k in range(K1)]
    LOADS += [("w2", k, W2K) for k in range(0, K2, W2K)]
    LOADS += [("w3", k, W3K) for k in range(0, K3, W3K)]
    SLOTS = 2
    W1_SPLIT, W2_SPLIT, W3_SPLIT = K1, K1 + K2 // W2K, len(LOADS)

    ctx = ExitStack()
    with ctx:
        def sb(name, shape, dt=F32):
            return ctx.enter_context(nc.sbuf_tensor(name, shape, dt))

        def pb(name):
            return ctx.enter_context(nc.psum_tensor(name, [P, 512], F32))

        def sem(name):
            return ctx.enter_context(nc.semaphore(name))

        w1_hi, w1_lo = sb("w1_hi", [P, K1, W1C], F32R), sb("w1_lo", [P, K1, W1C], F32R)
        w2_hi, w2_lo = sb("w2_hi", [P, K2, N2], F32R), sb("w2_lo", [P, K2, N2], F32R)
        w3_hi, w3_lo = sb("w3_hi", [P, K3, N3], F32R), sb("w3_lo", [P, K3, N3], F32R)
        stage = sb("stage", [P, SLOTS, STAGE])
        b1_rows, b2_rows, b3_rows = sb("b1_rows", [P, N1]), sb("b2_rows", [P, N2]), sb("b3_rows", [P, N3])
        out_w_rows = sb("out_w_rows", [P, N3])
        out_b_rows = sb("out_b_rows", [P, 1])
        x_raw = sb("x_raw", [P, D])
        xT_hi, xT_lo = sb("xT_hi", [P, K1, P], F32R), sb("xT_lo", [P, K1, P], F32R)
        h1 = sb("h1", [P, N1])
        h1T_hi, h1T_lo = sb("h1T_hi", [P, K2, P], F32R), sb("h1T_lo", [P, K2, P], F32R)
        h2 = sb("h2", [P, N2])
        h2T_hi, h2T_lo = sb("h2T_hi", [P, K3, P], F32R), sb("h2T_lo", [P, K3, P], F32R)
        h3 = sb("h3", [P, N3])
        ids = sb("ids", [P, TILES * F], I32)
        idx = sb("idx", [P, TILES * F], I32)
        tile_idx = sb("tile_idx", [P, F], I32)
        clamped, wrap = h1[:, 0:TILES * F], h1[:, 512:512 + TILES * F]
        VR = (2 * CROSS + 1) * K1
        vec_rows = sb("vec_rows", [VR, P])
        vec_cols = sb("vec_cols", [P, VR])
        identity = sb("identity", [P, P])
        ones = sb("ones", [P, P])
        bias_sums = sb("bias_sums", [P, CROSS, K1])
        products = sb("products", [P, K1])
        partials = sb("partials", [P, CROSS])
        consts = sb("consts", [P, CROSS])
        dots = sb("dots", [P, TILES, VECS])
        h3_dots = sb("h3_dots", [P, TILES])
        scale = sb("scale", [P, TILES])
        term = sb("term", [P, TILES])
        logits = sb("logits", [P, TILES])
        result = sb("result", [P, TILES])
        table = sb("table", [P, 1])

        l1_bank = [pb(f"l1_bank{i}") for i in range(3)]
        l23_bank = pb("l23_bank")
        x_bank = [pb(f"x_bank{i}") for i in range(2)]
        h_bank = [pb(f"h_bank{i}") for i in range(2)]

        ids_loaded = sem("ids_loaded")
        vecs_loaded = sem("vecs_loaded")
        rows_loaded = sem("rows_loaded")
        stage_loaded = [sem(f"stage_loaded{i}") for i in range(SLOTS)]
        hi_split = sem("hi_split")
        weights_split = sem("weights_split")
        identity_set = sem("identity_set")
        ones_set = sem("ones_set")
        vecs_transposed = sem("vecs_transposed")
        vec_cols_ready = sem("vec_cols_ready")
        cross_hi_ready = sem("cross_hi_ready")
        cross_ready = sem("cross_ready")
        partials_ready = sem("partials_ready")
        consts_summed = sem("consts_summed")
        gathered = [sem(f"gathered{g}") for g in range(NG)]
        gather_begun = sem("gather_begun")
        idx_ready = sem("idx_ready")
        x_transposed = sem("x_transposed")
        xT_hi_ready = sem("xT_hi_ready")
        xT_ready = sem("xT_ready")
        l1_done = sem("l1_done")
        h1_ready = sem("h1_ready")
        h1_transposed = sem("h1_transposed")
        h1T_hi_ready = sem("h1T_hi_ready")
        h1T_ready = sem("h1T_ready")
        l2_done = sem("l2_done")
        h2_ready = sem("h2_ready")
        h2_transposed = sem("h2_transposed")
        h2T_hi_ready = sem("h2T_hi_ready")
        h2T_ready = sem("h2T_ready")
        l3_done = sem("l3_done")
        h3_ready = sem("h3_ready")
        h3_read = sem("h3_read")
        chained = sem("chained")
        logits_ready = sem("logits_ready")
        result_ready = sem("result_ready")
        stored = sem("stored")

        block = ctx.enter_context(nc.Block())

        @block.sync
        def _(sync):
            sync.dma_start(ids[:, :], r_ids.rearrange("(p t) f -> p (t f)", p=P)).then_inc(ids_loaded, 16)
            for n, (name, k, m) in enumerate(LOADS):
                if n >= SLOTS:
                    sync.wait_ge(weights_split, n - SLOTS + 1)
                src = {"w1": w1, "w2": w2, "w3": w3}[name][k * P:(k + m) * P, :]
                dst = stage[:, n % SLOTS, :]
                if m > 1:
                    src = src.rearrange("(m p) c -> p m c", m=m)
                    dst = dst.rearrange("p (m c) -> p m c", m=m)
                sync.dma_start(dst, src).then_inc(stage_loaded[n % SLOTS], 16)
            sync.wait_ge(result_ready, 1)
            sync.dma_start(out[:, 0].rearrange("(p t) -> p t", p=P), result[:, :]).then_inc(stored, 16)
            sync.wait_ge(stored, 16)

        @block.gpsimd
        def _(pool):
            pool.memset(identity[:, :], 0.0).then_inc(identity_set, 1)
            pool.wait_ge(identity_set, 1)
            pool.affine_select(out=identity[:, :], in_=identity[:, :], compare_op=ALU.not_equal, fill=1.0,
                               base=0, pattern=[[-1, P]], channel_multiplier=1).then_inc(identity_set, 1)
            pool.memset(ones[:, :], 1.0).then_inc(ones_set, 1)
            with pool.Fori(0, TILES) as t:
                for g in range(NG):
                    pool.wait_ge(idx_ready, NG * t + g + 1)
                    pool.sem_inc(gather_begun, 1)
                    for f in range(F0[g], F0[g] + NF[g]):
                        pool.indirect_dma_start(
                            out=x_raw[:, f * E:(f + 1) * E], out_offset=None, in_=emb,
                            in_offset=bass.IndirectOffsetOnAxis(ap=tile_idx[:, f:f + 1], axis=0),
                        ).then_inc(gathered[g], 16)

        @block.scalar
        def _(act):
            act.dma_start(vec_rows[0:CROSS * K1, :], cross_w.rearrange("v (k p) -> (v k) p", p=P)).then_inc(vecs_loaded, 16)
            act.dma_start(vec_rows[CROSS * K1:VECS * K1, :],
                          out_w[0:D, 0].rearrange("(k p) -> k p", p=P)).then_inc(vecs_loaded, 16)
            act.dma_start(vec_rows[VECS * K1:VR, :], cross_b.rearrange("v (k p) -> (v k) p", p=P)).then_inc(vecs_loaded, 16)
            for rows, src in ((b1_rows, b1), (b2_rows, b2), (b3_rows, b3), (out_b_rows, out_b)):
                act.dma_start(rows[:, :], src.rearrange("(o n) -> o n", o=1).broadcast_to([P, src.shape[0]])).then_inc(rows_loaded, 16)
            act.dma_start(out_w_rows[:, :],
                          out_w[D:D + N3, 0].rearrange("(o n) -> o n", o=1).broadcast_to([P, N3])).then_inc(rows_loaded, 16)
            act.wait_ge(ones_set, 1)
            act.activation(table[:, :], ones[:, 0:1], ACT.Sigmoid)

            def split_hi(n):
                name, k, m = LOADS[n]
                act.wait_ge(stage_loaded[n % SLOTS], 16 * (n // SLOTS + 1))
                dst = {"w1": w1_hi, "w2": w2_hi, "w3": w3_hi}[name][:, k:k + m, 0:STAGE // m]
                src = stage[:, n % SLOTS, :].rearrange("p (m c) -> p m c", m=m)
                act.activation(dst, src, ACT.Copy).then_inc(hi_split, 1)

            def x_hi(t, g):
                act.wait_ge(x_transposed, NG * t + g + 1)
                ks, n = GROUPS[g], len(GROUPS[g])
                act.activation(xT_hi[:, ks[0]:ks[0] + n, :].rearrange("p k b -> p (k b)"),
                               x_bank[g % 2][:, 0:n * P], ACT.Copy).then_inc(xT_hi_ready, 1)

            def h1_hi(t):
                for half in range(2):
                    act.wait_ge(h1_transposed, 2 * t + half + 1)
                    act.activation(h1T_hi[:, half * HB:(half + 1) * HB, :].rearrange("p k b -> p (k b)"),
                                   h_bank[half][:, 0:HB * P], ACT.Relu).then_inc(h1T_hi_ready, 1)

            def h2_hi(t):
                act.wait_ge(h2_transposed, t + 1)
                act.activation(h2T_hi[:, :, :].rearrange("p k b -> p (k b)"), h_bank[0][:, 0:K3 * P],
                               ACT.Relu).then_inc(h2T_hi_ready, 1)

            def step(t, first=False, second=False, last=False):
                for g in range(NG):
                    if first:
                        for k in GROUPS[g]:
                            split_hi(k)
                        if g == 0:
                            x_hi(0, 0)
                    if g < NG - 1:
                        x_hi(t, g + 1)
                    elif first:
                        for n in range(W1_SPLIT, len(LOADS)):
                            split_hi(n)
                        x_hi(t + 1, 0)
                    elif not last:
                        x_hi(t + 1, 0)
                    if g == 0 and not first and not second:
                        h2_hi(t - 2)
                h1_hi(t)

            act.wait_ge(vecs_transposed, 1)
            act.activation(vec_cols[:, :], h_bank[0][:, 0:VR], ACT.Copy).then_inc(vec_cols_ready, 1)
            act.wait_ge(vec_cols_ready, 1)
            act.activation(w1_hi[:, :, N1:W1C], vec_cols[:, 0:VECS * K1].rearrange("p (v k) -> p k v", v=VECS),
                           ACT.Copy).then_inc(cross_hi_ready, 1)
            step(0, first=True)
            step(1, second=True)
            with act.Fori(2, TILES - 1) as t:
                step(t)
            step(TILES - 1, last=True)
            h2_hi(TILES - 2)
            h2_hi(TILES - 1)
            act.wait_ge(logits_ready, 1)
            act.activation(result[:, :], logits[:, :], ACT.Sigmoid).then_inc(result_ready, 1)

        @block.vector
        def _(dve):
            links = [0]

            def link(instruction):
                links[0] += 1
                instruction.then_inc(chained, 1)
                dve.wait_ge(chained, links[0])

            def split_lo(n):
                name, k, m = LOADS[n]
                dve.wait_ge(hi_split, n + 1)
                hi, lo = {"w1": (w1_hi, w1_lo), "w2": (w2_hi, w2_lo), "w3": (w3_hi, w3_lo)}[name]
                src = stage[:, n % SLOTS, :].rearrange("p (m c) -> p m c", m=m)
                dve.tensor_tensor(lo[:, k:k + m, 0:STAGE // m], src, hi[:, k:k + m, 0:STAGE // m].bitcast(F32),
                                  ALU.subtract).then_inc(weights_split, 1)

            def copy_idx(t, g):
                dve.tensor_copy(tile_idx[:, F0[g]:F0[g] + NF[g]], idx[:, bass.ds(t * F + F0[g], NF[g])]).then_inc(idx_ready, 1)

            def x_lo(t, g, next_tile=True):
                dve.wait_ge(xT_hi_ready, NG * t + g + 1)
                ks, n = GROUPS[g], len(GROUPS[g])
                dve.tensor_tensor(xT_lo[:, ks[0]:ks[0] + n, :].rearrange("p k b -> p (k b)"), x_bank[g % 2][:, 0:n * P],
                                  xT_hi[:, ks[0]:ks[0] + n, :].rearrange("p k b -> p (k b)").bitcast(F32),
                                  ALU.subtract).then_inc(xT_ready, 1)
                if next_tile:
                    copy_idx(t + 1, g)

            def relu_lo(bank, cols, hi, lo, done):
                dve.scalar_tensor_tensor(out=lo, in0=bank[:, 0:cols], scalar=0.0, in1=hi.bitcast(F32),
                                         op0=ALU.max, op1=ALU.subtract).then_inc(done, 1)

            def l1_out(t):
                dve.wait_ge(l1_done, t + 1)
                for (a, b), bank in zip(PIECES, l1_bank):
                    e = min(b, N1)
                    last = dve.tensor_tensor(h1[:, a:e], bank[:, 0:e - a], b1_rows[:, a:e], ALU.add)
                a = PIECES[-1][0]
                dve.tensor_copy(dots[:, bass.ds(t, 1), :].rearrange("p t v -> p (t v)"),
                                l1_bank[-1][:, N1 - a:W1C - a]).then_inc(h1_ready, 1)

            def l2_out(t):
                dve.wait_ge(l2_done, t + 1)
                dve.tensor_tensor(h2[:, :], l23_bank[:, 0:N2], b2_rows[:, :], ALU.add).then_inc(h2_ready, 1)

            def l3_out(t):
                dve.wait_ge(l3_done, t + 1)
                dve.tensor_tensor(h3[:, :], l23_bank[:, 0:N3], b3_rows[:, :], ALU.add).then_inc(h3_ready, 1)
                dve.wait_ge(h3_ready, t + 1)
                dve.scalar_tensor_tensor(out=h3[:, :], in0=h3[:, :], scalar=0.0, in1=out_w_rows[:, :], op0=ALU.max,
                                         op1=ALU.mult, accum_out=h3_dots[:, bass.ds(t, 1)]).then_inc(h3_read, 1)

            def h1_lo(t):
                for half in range(2):
                    dve.wait_ge(h1T_hi_ready, 2 * t + half + 1)
                    part = slice(half * HB, (half + 1) * HB)
                    relu_lo(h_bank[half], HB * P, h1T_hi[:, part, :].rearrange("p k b -> p (k b)"),
                            h1T_lo[:, part, :].rearrange("p k b -> p (k b)"), h1T_ready)

            def h2_lo(t):
                dve.wait_ge(h2T_hi_ready, t + 1)
                relu_lo(h_bank[0], K3 * P, h2T_hi[:, :, :].rearrange("p k b -> p (k b)"),
                        h2T_lo[:, :, :].rearrange("p k b -> p (k b)"), h2T_ready)

            def cross_consts():
                b = vec_cols[:, VECS * K1:VR].rearrange("p (v k) -> p v k", v=CROSS)
                link(dve.tensor_copy(bias_sums[:, 0, :], b[:, 0, :]))
                for i in range(1, CROSS):
                    link(dve.tensor_tensor(bias_sums[:, i, :], bias_sums[:, i - 1, :], b[:, i, :], ALU.add))
                for i in range(CROSS):
                    link(dve.tensor_tensor_reduce(out=products[:, :], in0=bias_sums[:, i, :],
                                                  in1=vec_cols[:, (i + 1) * K1:(i + 2) * K1], scale=1.0, scalar=0.0,
                                                  op0=ALU.mult, op1=ALU.add, accum_out=partials[:, i:i + 1]))
                dve.tensor_copy(products[:, 0:1], partials[:, 0:1]).then_inc(partials_ready, 1)
                dve.wait_ge(consts_summed, 1)
                link(dve.tensor_copy(consts[:, :], h_bank[1][:, 0:CROSS]))

            def step(t, first=False, second=False, before_last=False, last=False):
                for g in range(NG):
                    if first:
                        for k in GROUPS[g]:
                            split_lo(k)
                        if g == 0:
                            x_lo(0, 0)
                    if g < NG - 1:
                        x_lo(t, g + 1, next_tile=not last)
                    elif first:
                        for n in range(W1_SPLIT, len(LOADS)):
                            split_lo(n)
                        x_lo(t + 1, 0)
                    elif not last:
                        x_lo(t + 1, 0, next_tile=not before_last)
                    if g == 0 and not first and not second:
                        h2_lo(t - 2)
                    if g == 1 and not first and not second:
                        l3_out(t - 2)
                l1_out(t)
                if not first:
                    l2_out(t - 1)
                h1_lo(t)

            dve.wait_ge(ids_loaded, 16)
            link(dve.tensor_scalar(clamped, ids[:, :], float(-H), float(H - 1), ALU.max, ALU.min))
            link(dve.tensor_scalar(wrap, clamped, 0.0, float(H), ALU.is_lt, ALU.mult))
            link(dve.tensor_tensor(idx[:, :], clamped, wrap, ALU.add))
            for g in range(NG):
                copy_idx(0, g)
            dve.wait_ge(cross_hi_ready, 1)
            dve.tensor_tensor(w1_lo[:, :, N1:W1C], vec_cols[:, 0:VECS * K1].rearrange("p (v k) -> p k v", v=VECS),
                              w1_hi[:, :, N1:W1C].bitcast(F32), ALU.subtract).then_inc(cross_ready, 1)
            cross_consts()
            dve.wait_ge(rows_loaded, 5 * 16)
            step(0, first=True)
            step(1, second=True)
            T = TILES - 1
            with dve.Fori(2, T - 1) as t:
                step(t)
            step(T - 1, before_last=True)
            step(T, last=True)
            h2_lo(T - 1)
            l3_out(T - 1)
            l2_out(T)
            h2_lo(T)
            l3_out(T)
            link(dve.tensor_scalar(scale[:, :], dots[:, :, 0], 1.0, None, ALU.add))
            for i in range(1, CROSS):
                link(dve.tensor_tensor(term[:, :], scale[:, :], dots[:, :, i], ALU.mult))
                link(dve.scalar_tensor_tensor(out=scale[:, :], in0=term[:, :], scalar=consts[:, i - 1:i], in1=scale[:, :],
                                              op0=ALU.add, op1=ALU.add))
            link(dve.tensor_tensor(term[:, :], scale[:, :], dots[:, :, CROSS], ALU.mult))
            dve.wait_ge(h3_read, TILES)
            link(dve.scalar_tensor_tensor(out=term[:, :], in0=term[:, :], scalar=consts[:, CROSS - 1:CROSS],
                                          in1=h3_dots[:, :], op0=ALU.add, op1=ALU.add))
            dve.tensor_scalar(logits[:, :], term[:, :], out_b_rows[:, 0:1], None, ALU.add).then_inc(logits_ready, 1)

        @block.tensor
        def _(pe):
            def three_passes(bank_of, hi, lo, w_hi, w_lo, k, last_k):
                for n, (x, w) in enumerate(((hi, w_hi), (hi, w_lo), (lo, w_hi))):
                    for bank, a, b in bank_of:
                        done = pe.matmul(bank[:, 0:b - a], x[:, k, :], w[:, k, a:b],
                                         start=(k == 0 and n == 0), stop=(k == last_k and n == 2))
                return done

            def transpose_x(t, g):
                if not (isinstance(t, int) and NG * t + g < 2):
                    pe.wait_ge(xT_ready, NG * t + g - 1)
                pe.wait_ge(gathered[g], 16 * NF[g] * (t + 1))
                for i, k in enumerate(GROUPS[g]):
                    done = pe.transpose(x_bank[g % 2][:, i * P:(i + 1) * P], x_raw[:, k * P:(k + 1) * P], identity[:, :])
                done.then_inc(x_transposed, 1)

            def l1(t, g, first=False):
                if g == 0 and not first:
                    pe.wait_ge(h1_ready, t)
                pe.wait_ge(xT_ready, NG * t + g + 1)
                for k in GROUPS[g]:
                    if first:
                        pe.wait_ge(weights_split, k + 1)
                    done = three_passes([(l1_bank[i], a, b) for i, (a, b) in enumerate(PIECES)],
                                        xT_hi, xT_lo, w1_hi, w1_lo, k, K1 - 1)
                if g == NG - 1:
                    done.then_inc(l1_done, 1)

            def transpose_h1(t):
                pe.wait_ge(h1_ready, t + 1)
                for half in range(2):
                    for i in range(HB):
                        k = half * HB + i
                        done = pe.transpose(h_bank[half][:, i * P:(i + 1) * P], h1[:, k * P:(k + 1) * P], identity[:, :])
                    done.then_inc(h1_transposed, 1)

            def l2(t, first=False, reread=True):
                if first:
                    pe.wait_ge(weights_split, W2_SPLIT)
                if reread:
                    pe.wait_ge(h3_ready, t)
                pe.wait_ge(h1T_ready, 2 * t + 2)
                for k in range(K2):
                    done = three_passes([(l23_bank, 0, N2)], h1T_hi, h1T_lo, w2_hi, w2_lo, k, K2 - 1)
                done.then_inc(l2_done, 1)

            def transpose_h2(t):
                pe.wait_ge(h2_ready, t + 1)
                pe.wait_ge(h1T_ready, 2 * t + 3)
                transpose_h2_now()

            def transpose_h2_now():
                for i in range(K3):
                    done = pe.transpose(h_bank[0][:, i * P:(i + 1) * P], h2[:, i * P:(i + 1) * P], identity[:, :])
                done.then_inc(h2_transposed, 1)

            def l3(t):
                pe.wait_ge(h2T_ready, t + 1)
                for k in range(K3):
                    done = three_passes([(l23_bank, 0, N3)], h2T_hi, h2T_lo, w3_hi, w3_lo, k, K3 - 1)
                done.then_inc(l3_done, 1)

            def step(t, first=False, second=False, last=False):
                for g in range(NG):
                    if first:
                        l1(t, g, first)
                    if g < NG - 1:
                        transpose_x(t, g + 1)
                    elif not last:
                        transpose_x(t + 1, 0)
                    if not first:
                        l1(t, g)
                    if g == 0 and not first and not second:
                        transpose_h2(t - 2)
                    if g == 1 and not first and not second:
                        l3(t - 2)
                if not first:
                    l2(t - 1, first=second, reread=not second)
                transpose_h1(t)

            pe.wait_ge(identity_set, 2)
            pe.wait_ge(vecs_loaded, 3 * 16)
            pe.transpose(h_bank[0][:, 0:VR], vec_rows[:, :], identity[0:VR, 0:VR]).then_inc(vecs_transposed, 1)
            pe.wait_ge(ones_set, 1)
            pe.wait_ge(partials_ready, 1)
            pe.matmul(h_bank[1][:, 0:CROSS], ones[:, :], partials[:, :], start=True, stop=True).then_inc(consts_summed, 1)
            pe.wait_ge(cross_ready, 1)
            transpose_x(0, 0)
            step(0, first=True)
            step(1, second=True)
            with pe.Fori(2, TILES - 1) as t:
                step(t)
            T = TILES - 1
            step(T, last=True)
            transpose_h2(T - 1)
            l3(T - 1)
            l2(T)
            pe.wait_ge(h2_ready, T + 1)
            transpose_h2_now()
            l3(T)


_INS = ["r_ids", "L0_rec_emb", "L0_rec_cross_w", "L0_rec_cross_b", "L0_rec_w1", "L0_rec_b1", "L0_rec_w2", "L0_rec_b2",
        "L0_rec_w3", "L0_rec_b3", "L0_rec_out_w", "L0_rec_out_b"]


def kernel(**inputs):
    import numpy as _np
    import concourse.bacc as _bacc
    from concourse import mybir as _mybir
    from concourse.bass_utils import run_bass_kernel_spmd as _run

    nc = _bacc.Bacc("TRN2", target_bir_lowering=False, num_devices=1)
    arrays, args = {}, []
    for name in _INS:
        a = _np.ascontiguousarray(inputs[name])
        if a.ndim == 0:
            a = a.reshape(1)
        arrays[f"in_{name}"] = a
        args.append(nc.dram_tensor(f"in_{name}", a.shape, _mybir.dt.from_np(a.dtype), kind="ExternalInput").ap())
    rows = inputs["r_ids"].shape[0]
    args.append(nc.dram_tensor("out_0", (rows, 1), _mybir.dt.float32, kind="ExternalOutput").ap())
    dcn_ranker_kernel(nc, *args)
    r = _run(nc, [arrays], core_ids=[0])
    return r.results[0]["out_0"]
```

```python
import concourse.bass as bass
from concourse import mybir
from contextlib import ExitStack


def dcn_ranker_kernel(nc, r_ids, emb, cross_w, cross_b, w1, b1, w2, b2, w3, b3, out_w, out_b, out):
    F32 = mybir.dt.float32
    F32R = mybir.dt.float32r
    I32 = mybir.dt.int32
    ALU = mybir.AluOpType
    ACT = mybir.ActivationFunctionType

    P = 128
    B, F = r_ids.shape
    H, E = emb.shape
    D = F * E
    N1, N2, N3 = w1.shape[1], w2.shape[1], w3.shape[1]
    CROSS = cross_w.shape[0]
    TILES = B // P
    K1, K2, K3 = D // P, N1 // P, N2 // P
    VECS = CROSS + 1
    W1C = N1 + VECS
    FPK = P // E
    SIZES = [4, 4, 3, 2]
    NG = len(SIZES)
    GROUPS = [list(range(sum(SIZES[:g]), sum(SIZES[:g + 1]))) for g in range(NG)]
    assert sum(SIZES) == K1
    NF = [len(g) * FPK for g in GROUPS]
    F0 = [g[0] * FPK for g in GROUPS]
    cut = -(-W1C // 3)
    cut += cut % 2
    PIECES = [(0, cut), (cut, W1C - (W1C - cut) // 2), (W1C - (W1C - cut) // 2, W1C)]
    assert all((b - a) % 2 == 0 and 256 <= b - a <= 512 for a, b in PIECES)
    HB = N1 // P // 2
    assert N1 % P == 0 and N2 == 4 * P and N3 <= 512 and NG % 2 == 0 and HB * P <= 512

    STAGE = N1
    W2K, W3K = STAGE // N2, STAGE // N3
    LOADS = [("w1", k, 1) for k in range(K1)]
    LOADS += [("w2", k, W2K) for k in range(0, K2, W2K)]
    LOADS += [("w3", k, W3K) for k in range(0, K3, W3K)]
    SLOTS = 4
    W2_SPLIT = K1 + K2 // W2K
    SPLITS = [range(0, 5), range(5, 10), range(10, 14), range(14, len(LOADS))]
    assert all(GROUPS[g][-1] < SPLITS[g].stop for g in range(NG))

    ctx = ExitStack()
    with ctx:
        def sb(name, shape, dt=F32):
            return ctx.enter_context(nc.sbuf_tensor(name, shape, dt))

        def pb(name):
            return ctx.enter_context(nc.psum_tensor(name, [P, 512], F32))

        def sem(name):
            return ctx.enter_context(nc.semaphore(name))

        w1_hi, w1_lo = sb("w1_hi", [P, K1, W1C], F32R), sb("w1_lo", [P, K1, W1C], F32R)
        w2_hi, w2_lo = sb("w2_hi", [P, K2, N2], F32R), sb("w2_lo", [P, K2, N2], F32R)
        w3_hi, w3_lo = sb("w3_hi", [P, K3, N3], F32R), sb("w3_lo", [P, K3, N3], F32R)
        stage = sb("stage", [P, SLOTS, STAGE])
        h1, h2, h3 = stage[:, 2, :], stage[:, 3, 0:N2], stage[:, 3, N2:N2 + N3]
        b1_rows, b2_rows, b3_rows = sb("b1_rows", [P, N1]), sb("b2_rows", [P, N2]), sb("b3_rows", [P, N3])
        out_w_rows = sb("out_w_rows", [P, N3])
        out_b_rows = sb("out_b_rows", [P, 1])
        x_raw = sb("x_raw", [P, D])
        xT_hi, xT_lo = sb("xT_hi", [P, K1, P], F32R), sb("xT_lo", [P, K1, P], F32R)
        h1T_hi, h1T_lo = sb("h1T_hi", [P, K2, P], F32R), sb("h1T_lo", [P, K2, P], F32R)
        h2T_hi, h2T_lo = sb("h2T_hi", [P, K3, P], F32R), sb("h2T_lo", [P, K3, P], F32R)
        ids = sb("ids", [P, TILES * F], I32)
        idx = sb("idx", [P, TILES * F], I32)
        tile_idx = sb("tile_idx", [P, F], I32)
        assert D - 2 * TILES * F >= NF[0] * E
        clamped, wrap = x_raw[:, D - TILES * F:D], x_raw[:, D - 2 * TILES * F:D - TILES * F]
        VR = (2 * CROSS + 1) * K1
        vec_rows = sb("vec_rows", [VR, P])
        vec_cols = sb("vec_cols", [P, VR])
        identity = sb("identity", [P, P])
        ones = sb("ones", [P, P])
        bias_sums = sb("bias_sums", [P, CROSS, K1])
        products = sb("products", [P, K1])
        sums, partials = sb("sums", [P, CROSS]), sb("partials", [P, CROSS])
        consts = sb("consts", [P, CROSS])
        dots = sb("dots", [P, TILES, VECS])
        h3_dots = sb("h3_dots", [P, TILES])
        scale = sb("scale", [P, TILES])
        term = sb("term", [P, TILES])
        logits = sb("logits", [P, TILES])
        result = sb("result", [P, TILES])
        table = sb("table", [P, 1])

        l1_bank = [pb(f"l1_bank{i}") for i in range(3)]
        l2_bank = pb("l2_bank")
        x_bank = [pb(f"x_bank{i}") for i in range(2)]
        h_bank = [pb(f"h_bank{i}") for i in range(2)]
        l3_bank = h_bank[1]

        ids_loaded = sem("ids_loaded")
        vecs_loaded = sem("vecs_loaded")
        rows_loaded = sem("rows_loaded")
        stage_loaded = [sem(f"stage_loaded{i}") for i in range(SLOTS)]
        hi_split = sem("hi_split")
        weights_split = sem("weights_split")
        identity_set = sem("identity_set")
        ones_set = sem("ones_set")
        vecs_transposed = sem("vecs_transposed")
        vec_cols_ready = sem("vec_cols_ready")
        cross_hi_ready = sem("cross_hi_ready")
        cross_ready = sem("cross_ready")
        partials_ready = sem("partials_ready")
        consts_summed = sem("consts_summed")
        consts_ready = sem("consts_ready")
        gathered = [sem(f"gathered{g}") for g in range(NG)]
        gather_begun = sem("gather_begun")
        idx_ready = sem("idx_ready")
        x_transposed = sem("x_transposed")
        xT_hi_ready = sem("xT_hi_ready")
        xT_ready = sem("xT_ready")
        l1_done = sem("l1_done")
        h1_ready = sem("h1_ready")
        h1_transposed = sem("h1_transposed")
        h1T_hi_ready = sem("h1T_hi_ready")
        h1T_ready = sem("h1T_ready")
        l2_done = sem("l2_done")
        h2_ready = sem("h2_ready")
        h2_transposed = sem("h2_transposed")
        h2T_hi_ready = sem("h2T_hi_ready")
        h2T_ready = sem("h2T_ready")
        l3_done = sem("l3_done")
        h3_ready = sem("h3_ready")
        h3_read = sem("h3_read")
        chained = sem("chained")
        logits_ready = sem("logits_ready")
        result_ready = sem("result_ready")
        stored = sem("stored")

        block = ctx.enter_context(nc.Block())

        @block.sync
        def _(sync):
            sync.dma_start(ids[:, :], r_ids.rearrange("(p t) f -> p (t f)", p=P)).then_inc(ids_loaded, 16)
            for n, (name, k, m) in enumerate(LOADS):
                if n >= SLOTS:
                    sync.wait_ge(weights_split, n - SLOTS + 1)
                src = {"w1": w1, "w2": w2, "w3": w3}[name][k * P:(k + m) * P, :]
                dst = stage[:, n % SLOTS, :]
                if m > 1:
                    src = src.rearrange("(m p) c -> p m c", m=m)
                    dst = dst.rearrange("p (m c) -> p m c", m=m)
                sync.dma_start(dst, src).then_inc(stage_loaded[n % SLOTS], 16)
                if n == K1 - 1:
                    for rows, vec in ((b1_rows, b1), (b2_rows, b2), (b3_rows, b3), (out_w_rows, out_w[D:D + N3, 0]), (out_b_rows, out_b)):
                        sync.dma_start(rows[:, :], vec.rearrange("(o n) -> o n", o=1).broadcast_to([P, rows.shape[1]])).then_inc(rows_loaded, 16)
            sync.wait_ge(result_ready, 1)
            sync.dma_start(out[:, 0].rearrange("(p t) -> p t", p=P), result[:, :]).then_inc(stored, 16)
            sync.wait_ge(stored, 16)

        @block.gpsimd
        def _(pool):
            pool.memset(identity[:, :], 0.0).then_inc(identity_set, 1)
            pool.wait_ge(identity_set, 1)
            pool.affine_select(out=identity[:, :], in_=identity[:, :], compare_op=ALU.not_equal, fill=1.0,
                               base=0, pattern=[[-1, P]], channel_multiplier=1).then_inc(identity_set, 1)
            pool.memset(ones[:, :], 1.0).then_inc(ones_set, 1)
            with pool.Fori(0, TILES) as t:
                for g in range(NG):
                    pool.wait_ge(idx_ready, NG * t + g + 1)
                    pool.sem_inc(gather_begun, 1)
                    for f in range(F0[g], F0[g] + NF[g]):
                        pool.indirect_dma_start(
                            out=x_raw[:, f * E:(f + 1) * E], out_offset=None, in_=emb,
                            in_offset=bass.IndirectOffsetOnAxis(ap=tile_idx[:, f:f + 1], axis=0),
                        ).then_inc(gathered[g], 16)

        @block.scalar
        def _(act):
            act.dma_start(vec_rows[0:CROSS * K1, :], cross_w.rearrange("v (k p) -> (v k) p", p=P)).then_inc(vecs_loaded, 16)
            act.dma_start(vec_rows[CROSS * K1:VECS * K1, :],
                          out_w[0:D, 0].rearrange("(k p) -> k p", p=P)).then_inc(vecs_loaded, 16)
            act.dma_start(vec_rows[VECS * K1:VR, :], cross_b.rearrange("v (k p) -> (v k) p", p=P)).then_inc(vecs_loaded, 16)
            act.wait_ge(ones_set, 1)
            act.activation(table[:, :], ones[:, 0:1], ACT.Sigmoid)

            def split_hi(n):
                name, k, m = LOADS[n]
                act.wait_ge(stage_loaded[n % SLOTS], 16 * (n // SLOTS + 1))
                dst = {"w1": w1_hi, "w2": w2_hi, "w3": w3_hi}[name][:, k:k + m, 0:STAGE // m]
                src = stage[:, n % SLOTS, :].rearrange("p (m c) -> p m c", m=m)
                act.activation(dst, src, ACT.Copy).then_inc(hi_split, 1)

            def x_hi(t, g):
                act.wait_ge(x_transposed, NG * t + g + 1)
                ks, n = GROUPS[g], len(GROUPS[g])
                act.activation(xT_hi[:, ks[0]:ks[0] + n, :].rearrange("p k b -> p (k b)"),
                               x_bank[g % 2][:, 0:n * P], ACT.Copy).then_inc(xT_hi_ready, 1)

            def h1_hi(t):
                for half in range(2):
                    act.wait_ge(h1_transposed, 2 * t + half + 1)
                    act.activation(h1T_hi[:, half * HB:(half + 1) * HB, :].rearrange("p k b -> p (k b)"),
                                   h_bank[half][:, 0:HB * P], ACT.Relu).then_inc(h1T_hi_ready, 1)

            def h2_hi(t):
                act.wait_ge(h2_transposed, t + 1)
                act.activation(h2T_hi[:, :, :].rearrange("p k b -> p (k b)"), h_bank[0][:, 0:K3 * P],
                               ACT.Relu).then_inc(h2T_hi_ready, 1)

            def first_step():
                for g in range(NG):
                    for n in SPLITS[g]:
                        split_hi(n)
                    x_hi(0, g)
                h1_hi(0)
                x_hi(1, 0)

            def step(t, h2_of=None):
                x_hi(t, 1)
                if h2_of is not None:
                    h2_hi(h2_of)
                x_hi(t, 2)
                x_hi(t, 3)
                x_hi(t + 1, 0)
                h1_hi(t)

            def last_step(t):
                x_hi(t, 1)
                h2_hi(t - 2)
                x_hi(t, 2)
                x_hi(t, 3)
                h1_hi(t)
                h2_hi(t - 1)
                h2_hi(t)

            act.wait_ge(vecs_transposed, 1)
            act.activation(vec_cols[:, :], h_bank[0][:, 0:VR], ACT.Copy).then_inc(vec_cols_ready, 1)
            act.wait_ge(vec_cols_ready, 1)
            act.activation(w1_hi[:, :, N1:W1C], vec_cols[:, 0:VECS * K1].rearrange("p (v k) -> p k v", v=VECS),
                           ACT.Copy).then_inc(cross_hi_ready, 1)
            first_step()
            step(1)
            with act.Fori(2, TILES - 1) as t:
                step(t, h2_of=t - 2)
            last_step(TILES - 1)
            act.wait_ge(logits_ready, 1)
            act.activation(result[:, :], logits[:, :], ACT.Sigmoid).then_inc(result_ready, 1)

        @block.vector
        def _(dve):
            links = [0]

            def link(instruction):
                links[0] += 1
                instruction.then_inc(chained, 1)
                dve.wait_ge(chained, links[0])

            def split_lo(n):
                name, k, m = LOADS[n]
                dve.wait_ge(hi_split, n + 1)
                hi, lo = {"w1": (w1_hi, w1_lo), "w2": (w2_hi, w2_lo), "w3": (w3_hi, w3_lo)}[name]
                src = stage[:, n % SLOTS, :].rearrange("p (m c) -> p m c", m=m)
                dve.tensor_tensor(lo[:, k:k + m, 0:STAGE // m], src, hi[:, k:k + m, 0:STAGE // m].bitcast(F32),
                                  ALU.subtract).then_inc(weights_split, 1)

            def copy_idx(t, g):
                dve.tensor_copy(tile_idx[:, F0[g]:F0[g] + NF[g]], idx[:, bass.ds(t * F + F0[g], NF[g])]).then_inc(idx_ready, 1)

            def x_lo(t, g, next_tile=True):
                dve.wait_ge(xT_hi_ready, NG * t + g + 1)
                ks, n = GROUPS[g], len(GROUPS[g])
                dve.tensor_tensor(xT_lo[:, ks[0]:ks[0] + n, :].rearrange("p k b -> p (k b)"), x_bank[g % 2][:, 0:n * P],
                                  xT_hi[:, ks[0]:ks[0] + n, :].rearrange("p k b -> p (k b)").bitcast(F32),
                                  ALU.subtract).then_inc(xT_ready, 1)
                if next_tile:
                    copy_idx(t + 1, g)

            def relu_lo(bank, cols, hi, lo, done):
                dve.scalar_tensor_tensor(out=lo, in0=bank[:, 0:cols], scalar=0.0, in1=hi.bitcast(F32),
                                         op0=ALU.max, op1=ALU.subtract).then_inc(done, 1)

            def l1_out(t):
                dve.wait_ge(l1_done, t + 1)
                for (a, b), bank in zip(PIECES, l1_bank):
                    e = min(b, N1)
                    dve.tensor_tensor(h1[:, a:e], bank[:, 0:e - a], b1_rows[:, a:e], ALU.add)
                a = PIECES[-1][0]
                dve.tensor_copy(dots[:, bass.ds(t, 1), :].rearrange("p t v -> p (t v)"),
                                l1_bank[-1][:, N1 - a:W1C - a]).then_inc(h1_ready, 1)

            def l2_out(t):
                dve.wait_ge(l2_done, t + 1)
                dve.tensor_tensor(h2[:, :], l2_bank[:, 0:N2], b2_rows[:, :], ALU.add).then_inc(h2_ready, 1)

            def l3_out(t):
                dve.wait_ge(l3_done, t + 1)
                dve.tensor_tensor(h3[:, :], l3_bank[:, 0:N3], b3_rows[:, :], ALU.add).then_inc(h3_ready, 1)
                dve.wait_ge(h3_ready, t + 1)
                dve.scalar_tensor_tensor(out=h3[:, :], in0=h3[:, :], scalar=0.0, in1=out_w_rows[:, :], op0=ALU.max,
                                         op1=ALU.mult, accum_out=h3_dots[:, bass.ds(t, 1)]).then_inc(h3_read, 1)

            def h1_lo(t):
                for half in range(2):
                    dve.wait_ge(h1T_hi_ready, 2 * t + half + 1)
                    part = slice(half * HB, (half + 1) * HB)
                    relu_lo(h_bank[half], HB * P, h1T_hi[:, part, :].rearrange("p k b -> p (k b)"),
                            h1T_lo[:, part, :].rearrange("p k b -> p (k b)"), h1T_ready)

            def h2_lo(t):
                dve.wait_ge(h2T_hi_ready, t + 1)
                relu_lo(h_bank[0], K3 * P, h2T_hi[:, :, :].rearrange("p k b -> p (k b)"),
                        h2T_lo[:, :, :].rearrange("p k b -> p (k b)"), h2T_ready)

            def cross_consts():
                b = vec_cols[:, VECS * K1:VR].rearrange("p (v k) -> p v k", v=CROSS)
                link(dve.tensor_copy(bias_sums[:, 0, :], b[:, 0, :]))
                for i in range(1, CROSS):
                    link(dve.tensor_tensor(bias_sums[:, i, :], bias_sums[:, i - 1, :], b[:, i, :], ALU.add))
                for i in range(CROSS):
                    link(dve.tensor_tensor_reduce(out=products[:, :], in0=bias_sums[:, i, :],
                                                  in1=vec_cols[:, (i + 1) * K1:(i + 2) * K1], scale=1.0, scalar=0.0,
                                                  op0=ALU.mult, op1=ALU.add, accum_out=sums[:, i:i + 1]))
                dve.tensor_copy(partials[:, :], sums[:, :]).then_inc(partials_ready, 1)

            def cross_logits():
                dve.wait_ge(consts_ready, 1)
                dve.wait_ge(h1_ready, TILES)
                link(dve.tensor_scalar(scale[:, :], dots[:, :, 0], 1.0, None, ALU.add))
                for i in range(1, CROSS):
                    link(dve.tensor_tensor(term[:, :], scale[:, :], dots[:, :, i], ALU.mult))
                    link(dve.scalar_tensor_tensor(out=scale[:, :], in0=term[:, :], scalar=consts[:, i - 1:i],
                                                  in1=scale[:, :], op0=ALU.add, op1=ALU.add))
                link(dve.tensor_tensor(scale[:, :], scale[:, :], dots[:, :, CROSS], ALU.mult))
                link(dve.tensor_scalar(term[:, :], scale[:, :], consts[:, CROSS - 1:CROSS], out_b_rows[:, 0:1], ALU.add, ALU.add))

            def first_step():
                for g in range(NG):
                    for n in SPLITS[g]:
                        split_lo(n)
                    if g == 0:
                        cross_consts()
                    x_lo(0, g)
                dve.wait_ge(consts_summed, 1)
                dve.tensor_copy(consts[:, :], h_bank[1][:, 0:CROSS]).then_inc(consts_ready, 1)
                dve.wait_ge(rows_loaded, 5 * 16)
                dve.wait_ge(weights_split, len(LOADS))
                l1_out(0)
                h1_lo(0)
                x_lo(1, 0)
                l2_out(0)

            def step(t, behind=True, before_last=False):
                x_lo(t, 1)
                if behind:
                    h2_lo(t - 2)
                x_lo(t, 2)
                if behind:
                    l3_out(t - 2)
                x_lo(t, 3)
                l1_out(t)
                x_lo(t + 1, 0, next_tile=not before_last)
                if behind:
                    l2_out(t - 1)
                h1_lo(t)

            def last_step(t):
                x_lo(t, 1, next_tile=False)
                h2_lo(t - 2)
                x_lo(t, 2, next_tile=False)
                l3_out(t - 2)
                x_lo(t, 3, next_tile=False)
                l1_out(t)
                l2_out(t - 1)
                h1_lo(t)
                h2_lo(t - 1)
                cross_logits()
                l2_out(t)
                l3_out(t - 1)
                h2_lo(t)
                l3_out(t)

            def to_indices(a, b):
                c, w = clamped[:, a:b], wrap[:, a:b]
                link(dve.tensor_scalar(c, ids[:, a:b], float(-H), float(H - 1), ALU.max, ALU.min))
                link(dve.tensor_scalar(w, c, 0.0, float(H), ALU.is_lt, ALU.mult))
                link(dve.tensor_tensor(idx[:, a:b], c, w, ALU.add))

            dve.wait_ge(ids_loaded, 16)
            to_indices(0, F)
            copy_idx(0, 0)
            to_indices(F, TILES * F)
            for g in range(1, NG):
                copy_idx(0, g)
            dve.wait_ge(cross_hi_ready, 1)
            dve.tensor_tensor(w1_lo[:, :, N1:W1C], vec_cols[:, 0:VECS * K1].rearrange("p (v k) -> p k v", v=VECS),
                              w1_hi[:, :, N1:W1C].bitcast(F32), ALU.subtract).then_inc(cross_ready, 1)
            T = TILES - 1
            first_step()
            step(1, behind=False)
            with dve.Fori(2, T - 1) as t:
                step(t)
            step(T - 1, before_last=True)
            last_step(T)
            dve.wait_ge(h3_read, TILES)
            dve.tensor_tensor(logits[:, :], term[:, :], h3_dots[:, :], ALU.add).then_inc(logits_ready, 1)

        @block.tensor
        def _(pe):
            def three_passes(bank_of, hi, lo, w_hi, w_lo, k, last_k):
                for n, (x, w) in enumerate(((hi, w_hi), (hi, w_lo), (lo, w_hi))):
                    for bank, a, b in bank_of:
                        done = pe.matmul(bank[:, 0:b - a], x[:, k, :], w[:, k, a:b],
                                         start=(k == 0 and n == 0), stop=(k == last_k and n == 2))
                return done

            def transpose_x(t, g):
                if not (isinstance(t, int) and NG * t + g < 2):
                    pe.wait_ge(xT_ready, NG * t + g - 1)
                pe.wait_ge(gathered[g], 16 * NF[g] * (t + 1))
                for i, k in enumerate(GROUPS[g]):
                    done = pe.transpose(x_bank[g % 2][:, i * P:(i + 1) * P], x_raw[:, k * P:(k + 1) * P], identity[:, :])
                done.then_inc(x_transposed, 1)

            def l1(t, g, part=slice(None), first=False):
                ks = GROUPS[g][part]
                if ks[0] == 0 and not first:
                    pe.wait_ge(h1_ready, t)
                pe.wait_ge(xT_ready, NG * t + g + 1)
                for k in ks:
                    if first:
                        pe.wait_ge(weights_split, k + 1)
                    done = three_passes([(l1_bank[i], a, b) for i, (a, b) in enumerate(PIECES)],
                                        xT_hi, xT_lo, w1_hi, w1_lo, k, K1 - 1)
                if ks[-1] == K1 - 1:
                    done.then_inc(l1_done, 1)

            def transpose_h1(t, l3_before=True):
                pe.wait_ge(h1_ready, t + 1)
                for half in range(2):
                    if half == 1 and l3_before:
                        pe.wait_ge(h3_ready, t - 1)
                    for i in range(HB):
                        k = half * HB + i
                        done = pe.transpose(h_bank[half][:, i * P:(i + 1) * P], h1[:, k * P:(k + 1) * P], identity[:, :])
                    done.then_inc(h1_transposed, 1)

            def l2(t, ks):
                pe.wait_ge(h1T_ready, 2 * t + 1 + ks[-1] // HB)
                for k in ks:
                    done = three_passes([(l2_bank, 0, N2)], h1T_hi, h1T_lo, w2_hi, w2_lo, k, K2 - 1)
                if ks[-1] == K2 - 1:
                    done.then_inc(l2_done, 1)

            def transpose_h2(t, bank_read=None):
                pe.wait_ge(h2_ready, t + 1)
                if bank_read is not None:
                    pe.wait_ge(h1T_ready, bank_read)
                for i in range(K3):
                    done = pe.transpose(h_bank[0][:, i * P:(i + 1) * P], h2[:, i * P:(i + 1) * P], identity[:, :])
                done.then_inc(h2_transposed, 1)

            def l3(t):
                pe.wait_ge(h2T_ready, t + 1)
                for k in range(K3):
                    done = three_passes([(l3_bank, 0, N3)], h2T_hi, h2T_lo, w3_hi, w3_lo, k, K3 - 1)
                done.then_inc(l3_done, 1)

            BODY, LAST = slice(0, -1), slice(-1, None)

            def first_step():
                transpose_x(0, 0)
                for g in range(NG):
                    l1(0, g, BODY, first=True)
                    if g < NG - 1:
                        transpose_x(0, g + 1)
                    l1(0, g, LAST, first=True)
                pe.wait_ge(ones_set, 1)
                pe.wait_ge(partials_ready, 1)
                pe.matmul(h_bank[1][:, 0:CROSS], ones[:, :], partials[:, :], start=True, stop=True).then_inc(consts_summed, 1)
                pe.wait_ge(consts_ready, 1)
                transpose_h1(0, l3_before=False)
                pe.wait_ge(weights_split, W2_SPLIT)
                l2(0, range(0, HB))
                transpose_x(1, 0)
                l2(0, range(HB, K2))
                l1(1, 0, BODY)

            L2_PARTS = [range(i * K2 // NG, (i + 1) * K2 // NG) for i in range(NG)]

            def second_step():
                t = 1
                for g in range(1, NG):
                    transpose_x(t, g)
                    l1(t, g - 1, LAST)
                    l1(t, g, BODY)
                transpose_x(t + 1, 0)
                l1(t, NG - 1, LAST)
                transpose_h1(t, l3_before=False)
                l1(t + 1, 0)

            def step(t):
                transpose_x(t, 1)
                transpose_h2(t - 2, bank_read=2 * t - 1)
                l2(t - 1, L2_PARTS[0])
                l1(t, 1)
                transpose_x(t, 2)
                l3(t - 2)
                l2(t - 1, L2_PARTS[1])
                l1(t, 2)
                transpose_x(t, 3)
                l2(t - 1, L2_PARTS[2])
                l1(t, 3)
                transpose_x(t + 1, 0)
                l2(t - 1, L2_PARTS[3])
                transpose_h1(t)
                l1(t + 1, 0)

            def last_step(t):
                transpose_x(t, 1)
                transpose_h2(t - 2, bank_read=2 * t - 1)
                l2(t - 1, L2_PARTS[0])
                l1(t, 1)
                transpose_x(t, 2)
                l3(t - 2)
                l2(t - 1, L2_PARTS[1])
                l1(t, 2)
                transpose_x(t, 3)
                l2(t - 1, L2_PARTS[2])
                l1(t, 3)
                l2(t - 1, L2_PARTS[3])
                transpose_h1(t)
                pe.wait_ge(h2_ready, t)
                l2(t, range(0, HB))
                transpose_h2(t - 1, bank_read=2 * t + 1)
                l2(t, range(HB, K2))
                l3(t - 1)
                transpose_h2(t)
                pe.wait_ge(h3_ready, t)
                l3(t)

            pe.wait_ge(identity_set, 2)
            pe.wait_ge(vecs_loaded, 3 * 16)
            pe.transpose(h_bank[0][:, 0:VR], vec_rows[:, :], identity[0:VR, 0:VR]).then_inc(vecs_transposed, 1)
            pe.wait_ge(cross_ready, 1)
            first_step()
            second_step()
            with pe.Fori(2, TILES - 1) as t:
                step(t)
            last_step(TILES - 1)


_INS = ["r_ids", "L0_rec_emb", "L0_rec_cross_w", "L0_rec_cross_b", "L0_rec_w1", "L0_rec_b1", "L0_rec_w2", "L0_rec_b2",
        "L0_rec_w3", "L0_rec_b3", "L0_rec_out_w", "L0_rec_out_b"]


def kernel(**inputs):
    import numpy as _np
    import concourse.bacc as _bacc
    from concourse import mybir as _mybir
    from concourse.bass_utils import run_bass_kernel_spmd as _run

    nc = _bacc.Bacc("TRN2", target_bir_lowering=False, num_devices=1)
    arrays, args = {}, []
    for name in _INS:
        a = _np.ascontiguousarray(inputs[name])
        if a.ndim == 0:
            a = a.reshape(1)
        arrays[f"in_{name}"] = a
        args.append(nc.dram_tensor(f"in_{name}", a.shape, _mybir.dt.from_np(a.dtype), kind="ExternalInput").ap())
    rows = inputs["r_ids"].shape[0]
    args.append(nc.dram_tensor("out_0", (rows, 1), _mybir.dt.float32, kind="ExternalOutput").ap())
    dcn_ranker_kernel(nc, *args)
    r = _run(nc, [arrays], core_ids=[0])
    return r.results[0]["out_0"]
```
